# Optimizing a Trainium2 kernel written in Bass

```python
import numpy as np
import jax
import jax.numpy as jnp

def _softmax(x, axis=-1):
    return jax.nn.softmax(x, axis=axis)
def _gelu(x):
    return jax.nn.gelu(x, approximate=True)
def _silu(x):
    return jax.nn.silu(x)
def _sigmoid(x):
    return jax.nn.sigmoid(x)
def _layernorm(x, axis=-1, eps=1e-5):
    m = jnp.mean(x, axis=axis, keepdims=True)
    v = jnp.var(x, axis=axis, keepdims=True)
    return (x - m) / jnp.sqrt(v + eps)
def _scatter_add(tgt, idx, src, axis=0):
    return tgt.at[idx].add(src)
def _segment_sum(src, seg, n):
    return jax.ops.segment_sum(src, seg, n)

kernel_name = 'mk_metaformer_d1_conv_nhwc128_9d13c5'

def setup_inputs(seed: int = 0):
    np.random.seed(seed)
    _w = jnp.asarray
    def _rec_inputs():
        import jax
        import jax.numpy as jnp
        _gk = jax.random.key(seed)
        x = -0.0003929 + 0.9999 * jax.random.normal(jax.random.fold_in(_gk, 1), (4, 256, 128, 128), jnp.float32)
        return x
    x = _rec_inputs()
    def _L0_conv_setup():
        import jax, jax.numpy as jnp
        import numpy as np
        C = 256
        NH = 16
        HD = C // NH
        H = 128
        W = 128
        N = 4
        D = float(np.sqrt(C))

        def _conv1x1(w, x):
            return jnp.einsum('oc,nchw->nohw', w, x)
        key = jax.random.key(seed)
        ks = jax.random.split(key, 12)
        u = lambda k, s: jax.random.uniform(k, s, jnp.float32, 0.1, 0.9)
        nrm = lambda k, s: jax.random.normal(k, s, jnp.float32) * 0.02
        return {'x': jax.random.normal(ks[0], (N, C, H, W), jnp.float32), 'wq': nrm(ks[1], (C, C)), 'wk': nrm(ks[2], (C, C)), 'wv': nrm(ks[3], (C, C)), 'wo': nrm(ks[4], (C, C)), 'rq': u(ks[5], (NH, HD, W, W)), 'rk': u(ks[6], (NH, HD, W, W)), 'rv': u(ks[7], (NH, HD, W, W)), 'Gq': u(ks[8], (NH, 1, 1, 1)), 'Gk': u(ks[9], (NH, 1, 1, 1)), 'Gv1': u(ks[10], (NH, 1, 1, 1)), 'Gv2': u(ks[11], (NH, 1, 1, 1))}
    _L0_conv_all = _L0_conv_setup()
    _L0_conv_in = {k: v for k, v in _L0_conv_all.items() if k in ('wq', 'wk', 'wv', 'wo', 'rq', 'rk', 'rv', 'Gq', 'Gk', 'Gv1', 'Gv2', )}
    del _L0_conv_all

    def _L0_ffn_setup():
        import jax, jax.numpy as jnp
        import numpy as np
        B, S, D, E, H, O, K = (512, 2048, 128, 64, 512, 128, 8)
        key = jax.random.key(seed)
        k0, k1, k2, k3 = jax.random.split(key, 4)
        x = jax.random.normal(k0, (B, S, D), dtype=jnp.float32)
        gate_w = jax.random.normal(k1, (E, D), dtype=jnp.float32) * (1.0 / np.sqrt(D))
        gate_b = jnp.zeros((E,), dtype=jnp.float32)
        weight1 = jax.random.uniform(k2, (E, D + 1, H), dtype=jnp.float32, minval=-1.0, maxval=1.0) * (1.0 / np.sqrt(D + 1))
        weight2 = jax.random.uniform(k3, (E, H + 1, O), dtype=jnp.float32, minval=-1.0, maxval=1.0) * (1.0 / np.sqrt(H + 1))
        return {'x': x, 'gate_w': gate_w, 'gate_b': gate_b, 'weight1': weight1, 'weight2': weight2}
    _L0_ffn_all = _L0_ffn_setup()
    _L0_ffn_in = {k: v for k, v in _L0_ffn_all.items() if k in ('gate_w', 'gate_b', 'weight1', 'weight2', )}
    del _L0_ffn_all

    return {
        "x": x,
        "L0_conv_wq": _L0_conv_in["wq"],
        "L0_conv_wk": _L0_conv_in["wk"],
        "L0_conv_wv": _L0_conv_in["wv"],
        "L0_conv_wo": _L0_conv_in["wo"],
        "L0_conv_rq": _L0_conv_in["rq"],
        "L0_conv_rk": _L0_conv_in["rk"],
        "L0_conv_rv": _L0_conv_in["rv"],
        "L0_conv_Gq": _L0_conv_in["Gq"],
        "L0_conv_Gk": _L0_conv_in["Gk"],
        "L0_conv_Gv1": _L0_conv_in["Gv1"],
        "L0_conv_Gv2": _L0_conv_in["Gv2"],
        "L0_ffn_gate_w": _L0_ffn_in["gate_w"],
        "L0_ffn_gate_b": _L0_ffn_in["gate_b"],
        "L0_ffn_weight1": _L0_ffn_in["weight1"],
        "L0_ffn_weight2": _L0_ffn_in["weight2"],
    }

def reference(x, L0_conv_wq, L0_conv_wk, L0_conv_wv, L0_conv_wo, L0_conv_rq, L0_conv_rk, L0_conv_rv, L0_conv_Gq, L0_conv_Gk, L0_conv_Gv1, L0_conv_Gv2, L0_ffn_gate_w, L0_ffn_gate_b, L0_ffn_weight1, L0_ffn_weight2):
    import jax
    import jax.numpy as jnp
    def _L0_conv_ref(x, wq, wk, wv, wo, rq, rk, rv, Gq, Gk, Gv1, Gv2):
        import jax, jax.numpy as jnp
        import numpy as np
        C = 256
        NH = 16
        HD = C // NH
        H = 128
        W = 128
        N = 4
        D = float(np.sqrt(C))

        def _conv1x1(w, x):
            return jnp.einsum('oc,nchw->nohw', w, x)
        n = x.shape[0]
        q = _conv1x1(wq, x).reshape(n, NH, HD, H, W)
        k = _conv1x1(wk, x).reshape(n, NH, HD, H, W)
        v = _conv1x1(wv, x).reshape(n, NH, HD, H, W)
        qk = jnp.einsum('nhcij,nhciw->nhijw', q, k) / D
        qrq = jnp.einsum('nhcij,chjw->nhijw', q, rq) / D
        krk = jnp.einsum('nhcij,chjw->nhijw', k, rk) / D
        weight = jax.nn.softmax(qk + Gq * qrq + Gk * krk, axis=3)
        out = jnp.einsum('nhijw,nhciw->nhcij', weight, Gv1 * v) + jnp.einsum('nhijw,chjw->nhcij', weight, Gv2 * rv)
        out = out.reshape(n, C, H, W)
        return _conv1x1(wo, out)

    def _L0_ffn_ref(x, gate_w, gate_b, weight1, weight2):
        import jax, jax.numpy as jnp
        import numpy as np
        B, S, D, E, H, O, K = (512, 2048, 128, 64, 512, 128, 8)
        Bn, Sn, Dn = x.shape
        logits = jnp.einsum('bsd,ed->bse', x, gate_w) + gate_b
        probs = jax.nn.softmax(logits, axis=1)
        vals, idx = jax.lax.top_k(probs.transpose(0, 2, 1), K)
        topv = vals.transpose(0, 2, 1)
        topi = idx.transpose(0, 2, 1)
        flat_idx = topi.reshape(Bn, K * E)
        gathered = jnp.take_along_axis(x, flat_idx[:, :, None], axis=1)
        gathered = gathered.reshape(Bn, K, E, Dn)
        pooled = jnp.einsum('bked,bke->bed', gathered, topv)
        ones = jnp.ones((E, Bn, 1), dtype=x.dtype)
        h = jnp.concatenate([pooled.transpose(1, 0, 2), ones], axis=-1)
        h = jax.nn.gelu(jnp.einsum('ebd,edh->ebh', h, weight1), approximate=False)
        h = jnp.concatenate([h, ones], axis=-1)
        out = jnp.einsum('ebh,eho->ebo', h, weight2)
        out = out.transpose(1, 0, 2)
        weighted = jnp.einsum('beo,bke->bkeo', out, topv).reshape(Bn, K * E, O)
        outputs = jnp.zeros((Bn, Sn, O), dtype=x.dtype)
        outputs = outputs.at[jnp.arange(Bn)[:, None], flat_idx].add(weighted)
        return outputs

    def _gn(v, G=32, eps=1e-5):
        B_, H_, W_, C_ = v.shape
        g = v.reshape(B_, H_, W_, G, C_ // G)
        m = jnp.mean(g, axis=(1, 2, 4), keepdims=True)
        s = jnp.var(g, axis=(1, 2, 4), keepdims=True)
        return ((g - m) / jnp.sqrt(s + eps)).reshape(v.shape)

    def _ln_c(v, eps=1e-6):
        m = jnp.mean(v, axis=-1, keepdims=True)
        s = jnp.var(v, axis=-1, keepdims=True)
        return (v - m) / jnp.sqrt(s + eps)

    def _ln_t(v, eps=1e-5):
        m = jnp.mean(v, axis=-1, keepdims=True)
        s = jnp.var(v, axis=-1, keepdims=True)
        return (v - m) / jnp.sqrt(s + eps)

    def _to_tokens(v):
        B_, H_, W_, C_ = v.shape
        return v.reshape(B_, H_ * W_, C_)
    def _from_tokens(t, like):
        return t.reshape(like.shape)

    x = x + _L0_conv_ref(_ln_c(x), L0_conv_wq, L0_conv_wk, L0_conv_wv, L0_conv_wo, L0_conv_rq, L0_conv_rk, L0_conv_rv, L0_conv_Gq, L0_conv_Gk, L0_conv_Gv1, L0_conv_Gv2)
    t = _to_tokens(x)
    t = t + _L0_ffn_ref(_ln_t(t), L0_ffn_gate_w, L0_ffn_gate_b, L0_ffn_weight1, L0_ffn_weight2)
    x = _from_tokens(t, x)
    return x


_drawn_inputs = setup_inputs


def setup_inputs(seed=0):
    import zlib

    import numpy as np

    out = dict(_drawn_inputs(seed))
    spreads = {'L0_ffn_gate_b': (0.0, 0.1)}
    factors = {'L0_conv_wq': 8.0,
     'L0_conv_wk': 8.0,
     'L0_conv_wv': 8.0,
     'L0_conv_rq': 8.0,
     'L0_conv_rk': 8.0,
     'L0_conv_rv': 8.0,
     'L0_conv_Gq': 8.0,
     'L0_conv_Gk': 8.0,
     'L0_conv_Gv1': 8.0,
     'L0_ffn_gate_w': 8.0,
     'L0_ffn_weight1': 8.0,
     'L0_ffn_weight2': 8.0}
    for name, (base, spread) in spreads.items():
        noise = np.random.default_rng([zlib.crc32(name.encode()), seed]).standard_normal(out[name].shape)
        drawn = base * np.exp(spread * noise) if base else spread * noise
        out[name] = jnp.asarray(drawn.astype(out[name].dtype))
    for name, factor in factors.items():
        out[name] = (out[name] * factor).astype(out[name].dtype)
    return out
```

```python
from contextlib import ExitStack

import concourse.bass as bass
from concourse import mybir

P = 128
ALU = mybir.AluOpType
ACT = mybir.ActivationFunctionType
BF16 = mybir.dt.bfloat16
F32 = mybir.dt.float32
U32 = mybir.dt.uint32
AX_X = mybir.AxisListType.X

N, C, H, W = 4, 256, 128, 128
NH = 16
HD = C // NH
PIX = H * W
CHALF = C // P
PAIRS = 6
PARTS = 3
EXPERTS, TOPK, HID = 64, 8, 512
CONV_EPS, TOKEN_EPS = 1e-6, 1e-5
SCALE = float(C) ** -0.5
BANK = 512


class Scope:

    def __init__(self, nc, ctx, phase):
        self.nc, self.ctx, self.phase = nc, ctx, phase

    def sb(self, name, shape, dt=F32):
        return self.ctx.enter_context(self.nc.sbuf_tensor(f"{self.phase}_{name}", shape, dt))

    def ps(self, name, shape, dt=F32):
        return self.ctx.enter_context(self.nc.psum_tensor(f"{self.phase}_{name}", shape, dt))

    def sem(self, name):
        return self.ctx.enter_context(self.nc.semaphore(f"{self.phase}_{name}"))


def make_identity(pool, ident, ident_zero, ident_ready):
    pool.memset(ident[:, :], 0.0).then_inc(ident_zero, 1)
    pool.wait_ge(ident_zero, 1)
    pool.affine_select(out=ident[:, :], in_=ident[:, :], compare_op=ALU.not_equal, fill=1.0, base=0,
                       pattern=[[-1, ident.shape[1]]], channel_multiplier=1).then_inc(ident_ready, 1)


def prepare(nc, d):
    with ExitStack() as ctx:
        s = Scope(nc, ctx, "prep")
        XC = 2048
        CHUNKS = PIX // XC
        ident = s.sb("ident", [P, P])
        w_in = s.sb("w_in", [P, 4, CHALF, C])
        w_t = s.sb("w_t", [P, 4, CHALF, C])
        gain_v = s.sb("gain_v", [P, CHALF])
        gain_r = s.sb("gain_r", [P, 2])
        gain_rv = s.sb("gain_rv", [P, HD])
        r_in = [s.sb(f"r_in{u}", [P, XC]) for u in range(2)]
        r_rest = [s.sb(f"r_rest{u}", [P, XC]) for u in range(2)]
        r_out = [s.sb(f"r_out{u}", [P, PARTS, XC], BF16) for u in range(2)]
        rv_in = [s.sb(f"rv_in{u}", [P, HD, W]) for u in range(2)]
        rv_out = [s.sb(f"rv_out{u}", [P, W, HD]) for u in range(2)]
        w_ps = s.ps("w_ps", [P, 4, BANK])
        rv_ps = s.ps("rv_ps", [P, 4, BANK])
        ident_zero, ident_ready = s.sem("ident_zero"), s.sem("ident_ready")
        w_loaded, gains_loaded = s.sem("w_loaded"), s.sem("gains_loaded")
        v_scaled, w_turned, w_copied, stored_w = s.sem("v_scaled"), s.sem("w_turned"), s.sem("w_copied"), s.sem("stored_w")
        r_loaded = [s.sem(f"r_loaded{u}") for u in range(2)]
        r_scaled, r_high, r_left, r_mid, r_low = (s.sem(x) for x in ("r_scaled", "r_high", "r_left", "r_mid", "r_low"))
        r_stored = [s.sem(f"r_stored{u}") for u in range(2)]
        rv_loaded = [s.sem(f"rv_loaded{u}") for u in range(2)]
        rv_turned, rv_copied = s.sem("rv_turned"), s.sem("rv_copied")
        rv_stored = [s.sem(f"rv_stored{u}") for u in range(2)]
        block = ctx.enter_context(nc.Block())

        STEPS = 2 * CHALF * CHUNKS
        tables = [d["rq"].rearrange("(a c) h j w -> a (c h) (j w)", a=CHALF), d["rk"].rearrange("(a c) h j w -> a (c h) (j w)", a=CHALF)]

        parts = [d["r_parts"][t].rearrange("p (a c) h x -> a (c h) p x", a=CHALF) for t in range(2)]

        @block.sync
        def _(sp):
            for m, name in enumerate(("wq", "wk", "wv", "wo")):
                sp.dma_start(w_in[:, m], d[name].rearrange("(a o) c -> o a c", a=CHALF)).then_inc(w_loaded, 16)
            for a in range(CHALF):
                for g in range(P // HD):
                    sp.dma_start(gain_v[g * HD:(g + 1) * HD, a:a + 1],
                                 d["Gv1"][a * (NH // CHALF) + g].rearrange("a b c -> a (b c)").to_broadcast([HD, 1])).then_inc(gains_loaded, 16)
            for t, name in enumerate(("Gq", "Gk")):
                for g in range(P // NH):
                    sp.dma_start(gain_r[g * NH:(g + 1) * NH, t:t + 1], d[name].rearrange("a b c e -> a (b c e)")).then_inc(gains_loaded, 16)
            sp.dma_start(gain_rv[:, :], d["Gv2"].rearrange("h b c e -> (b c e) h").to_broadcast([P, HD])).then_inc(gains_loaded, 16)
            for t in range(2):
                for a in range(CHALF):
                    with sp.Fori(0, CHUNKS // 2) as i:
                        for u in range(2):
                            done = (t * CHALF + a) * (CHUNKS // 2) + i
                            sp.wait_ge(r_left, 2 * done + u + 1)
                            sp.dma_start(r_in[u][:, :], tables[t][a][:, bass.ds((2 * i + u) * XC, XC)]).then_inc(r_loaded[u], 16)
            with sp.Fori(0, NH // 2) as i:
                for u in range(2):
                    sp.wait_ge(rv_turned, 4 * (2 * i + u) + 4)
                    for j in (0, W // 2):
                        sp.dma_start(rv_in[u][j:j + W // 2, :, :], d["rv"][:, bass.ds(2 * i + u, 1), j:j + W // 2].rearrange("c h j w -> (h j) c w")).then_inc(rv_loaded[u], 16)
            sp.wait_ge(w_copied, 8)
            for m in range(4):
                sp.dma_start(d["w_t"][m].rearrange("(a c) o -> c a o", a=CHALF), w_t[:, m]).then_inc(stored_w, 16)
            sp.wait_ge(stored_w, 64)

        @block.scalar
        def _(act):
            act.sem_inc(r_left, 2)
            act.sem_inc(r_stored[0], 16)
            act.sem_inc(r_stored[1], 16)
            for t in range(2):
                for a in range(CHALF):
                    with act.Fori(0, CHUNKS // 2) as i:
                        for u in range(2):
                            k = 2 * ((t * CHALF + a) * (CHUNKS // 2) + i) + u
                            act.wait_ge(r_scaled, k + 1)
                            act.wait_ge(r_stored[u], 16 * ((t * CHALF + a) * (CHUNKS // 2) + i) + 16)
                            act.activation(r_out[u][:, 0], r_in[u][:, :], ACT.Copy).then_inc(r_high, 1)
                            act.wait_ge(r_left, k + 3)
                            act.activation(r_out[u][:, 1], r_rest[u][:, :], ACT.Copy).then_inc(r_mid, 1)
                        for u in range(2):
                            k = 2 * ((t * CHALF + a) * (CHUNKS // 2) + i) + u
                            act.wait_ge(r_low, k + 3)
                            act.dma_start(parts[t][a][:, :, bass.ds((2 * i + u) * XC, XC)], r_out[u][:, :, :]).then_inc(r_stored[u], 16)
            with act.Fori(0, NH // 2) as i:
                for u in range(2):
                    act.wait_ge(rv_copied, 4 * (2 * i + u) + 8)
                    act.dma_start(d["rv_t"][bass.ds(2 * i + u, 1)].rearrange("h w x -> (h w) x"),
                                  rv_out[u][:, :, :].rearrange("w j c -> w (j c)")).then_inc(rv_stored[u], 16)
            for u in range(2):
                act.wait_ge(r_stored[u], 16 * (STEPS // 2 + 1))
                act.wait_ge(rv_stored[u], 16 * (NH // 2 + 1))

        @block.vector
        def _(dve):
            for u in range(2):
                dve.sem_inc(rv_stored[u], 16)
            dve.sem_inc(rv_copied, 4)
            dve.wait_ge(gains_loaded, 16 * (CHALF * (P // HD) + 2 * (P // NH) + 1))
            dve.wait_ge(w_loaded, 64)
            for a in range(CHALF):
                dve.tensor_scalar(w_in[:, 2, a], w_in[:, 2, a], gain_v[:, a:a + 1], None, ALU.mult).then_inc(v_scaled, 1)
            dve.tensor_scalar(w_in[:, 0], w_in[:, 0], SCALE, None, ALU.mult).then_inc(v_scaled, 1)
            dve.tensor_scalar(gain_r[:, 1:2], gain_r[:, 1:2], SCALE, None, ALU.mult).then_inc(v_scaled, 1)
            dve.wait_ge(v_scaled, CHALF + 2)
            for t in range(2):
                with dve.Fori(0, STEPS // 4) as i:
                    for u in range(2):
                        k = t * (STEPS // 4) + i
                        dve.wait_ge(r_loaded[u], 16 * k + 16)
                        dve.tensor_scalar(r_in[u][:, :], r_in[u][:, :], gain_r[:, t:t + 1], None, ALU.mult).then_inc(r_scaled, 1)
                        dve.wait_ge(r_high, 2 * k + u + 1)
                        dve.wait_ge(r_low, 2 * k + u + 1)
                        dve.tensor_tensor(r_rest[u][:, :], r_in[u][:, :], r_out[u][:, 0], ALU.subtract).then_inc(r_left, 1)
            for b in range(8):
                m, a = b // 2, b % 2
                dve.wait_ge(w_turned, b + 1)
                dve.tensor_copy(w_t[:, m, a], w_ps[:, b % 4, 0:C]).then_inc(w_copied, 1)
            with dve.Fori(0, NH // 2) as i:
                for u in range(2):
                    for b in range(4):
                        dve.wait_ge(rv_turned, 4 * (2 * i + u) + b + 9)
                        if b == 0:
                            dve.wait_ge(rv_stored[u], 16 * i + 16)
                        for c in range(4):
                            last = dve.tensor_scalar(rv_out[u][:, :, 4 * b + c], rv_ps[:, b, c * P:(c + 1) * P],
                                                     gain_rv[:, 4 * b + c:4 * b + c + 1], None, ALU.mult)
                        last.then_inc(rv_copied, 1)

        @block.gpsimd
        def _(pool):
            make_identity(pool, ident, ident_zero, ident_ready)
            pool.sem_inc(r_low, 2)
            with pool.Fori(0, STEPS // 2) as i:
                for u in range(2):
                    pool.wait_ge(r_mid, 2 * i + u + 1)
                    pool.tensor_tensor(r_out[u][:, 2], r_rest[u][:, :], r_out[u][:, 1], ALU.subtract).then_inc(r_low, 1)

        @block.tensor
        def _(pe):
            pe.sem_inc(rv_turned, 8)
            pe.wait_ge(ident_ready, 1)
            pe.wait_ge(v_scaled, CHALF + 2)
            for b in range(8):
                m, a = b // 2, b % 2
                if b >= 4:
                    pe.wait_ge(w_copied, b - 3)
                for o in range(CHALF):
                    last = pe.transpose(w_ps[:, b % 4, o * P:(o + 1) * P], w_in[:, m, o, a * P:(a + 1) * P], ident[:, :])
                last.then_inc(w_turned, 1)
            with pe.Fori(0, NH // 2) as i:
                for u in range(2):
                    pe.wait_ge(rv_loaded[u], 32 * i + 32)
                    for b in range(4):
                        pe.wait_ge(rv_copied, 4 * (2 * i + u) + b + 1)
                        for c in range(4):
                            last = pe.transpose(rv_ps[:, b, c * P:(c + 1) * P], rv_in[u][:, 4 * b + c, :], ident[:, :])
                        last.then_inc(rv_turned, 1)


ROWS = 8
CHUNK = ROWS * W
NCHUNK = N * PIX // CHUNK
GROUPS = CHALF * ROWS


class LayerNorm:

    TICKS = 8

    def __init__(self, s, eps):
        self.eps = eps
        self.xc = s.sb("ln_xc", [P, GROUPS, W])
        self.sq = s.sb("ln_sq", [P, GROUPS, W])
        self.mean, self.var, self.std, self.inv, self.t = (s.sb(f"ln_{n}", [P, GROUPS]) for n in ("mean", "var", "std", "inv", "t"))
        self.tick, self.squared, self.rooted = s.sem("ln_tick"), s.sem("ln_squared"), s.sem("ln_rooted")

    def mean_of(self, dve, x, k):
        tick, base = self.tick, self.TICKS * k
        dve.tensor_reduce(self.t[:, :], x, AX_X, ALU.add).then_inc(tick, 1)
        dve.wait_ge(tick, base + 1)
        dve.tensor_scalar(self.mean[:, :], self.t[:, :], -1.0 / W, None, ALU.mult).then_inc(tick, 1)

    def centre(self, dve, x, k):
        tick, base = self.tick, self.TICKS * k
        dve.wait_ge(tick, base + 2)
        return dve.tensor_tensor(self.xc[:, :, :], x, self.mean[:, :].unsqueeze(2).broadcast_to([P, GROUPS, W]), ALU.add)

    def square(self, act, centred, count):
        act.wait_ge(centred, count)
        act.activation(self.sq[:, :, :], self.xc[:, :, :], ACT.Square).then_inc(self.squared, 1)

    def variance(self, dve, k):
        tick, base = self.tick, self.TICKS * k
        dve.wait_ge(self.squared, k + 1)
        dve.tensor_reduce(self.t[:, :], self.sq[:, :, :], AX_X, ALU.add).then_inc(tick, 1)
        dve.wait_ge(tick, base + 3)
        dve.tensor_scalar(self.var[:, :], self.t[:, :], 1.0 / W, self.eps, ALU.mult, ALU.add).then_inc(tick, 1)

    def root(self, act, k):
        act.wait_ge(self.tick, self.TICKS * k + 4)
        act.activation(self.std[:, :], self.var[:, :], ACT.Sqrt).then_inc(self.rooted, 1)

    def scale(self, dve, out, k):
        tick, base = self.tick, self.TICKS * k
        dve.wait_ge(self.rooted, k + 1)
        dve.reciprocal(self.inv[:, :], self.std[:, :]).then_inc(tick, 1)
        dve.wait_ge(tick, base + 5)
        dve.tensor_tensor(self.t[:, :], self.inv[:, :], self.inv[:, :], ALU.mult).then_inc(tick, 1)
        dve.wait_ge(tick, base + 6)
        dve.scalar_tensor_tensor(out=self.t[:, :], in0=self.t[:, :], scalar=-0.5, in1=self.var[:, :], op0=ALU.mult, op1=ALU.mult).then_inc(tick, 1)
        dve.wait_ge(tick, base + 7)
        dve.scalar_tensor_tensor(out=self.inv[:, :], in0=self.t[:, :], scalar=1.5, in1=self.inv[:, :], op0=ALU.add, op1=ALU.mult).then_inc(tick, 1)
        dve.wait_ge(tick, base + 8)
        return dve.tensor_tensor(out, self.xc[:, :, :], self.inv[:, :].unsqueeze(2).broadcast_to([P, GROUPS, W]), ALU.mult)


def pipelined(eng, steps, body):
    body(0, 0, True, False)
    body(1, 1, False, False)
    with eng.Fori(1, steps // 2 - 1) as i:
        for u in range(2):
            body(2 * i + u, u, False, False)
    body(steps - 2, 0, False, False)
    body(steps - 1, 1, False, True)


def project(nc, d):
    with ExitStack() as ctx:
        s = Scope(nc, ctx, "proj")
        TILES = 8
        x = [s.sb(f"x{u}", [P, GROUPS, W]) for u in range(2)]
        xn = [s.sb(f"xn{u}", [P, CHALF, CHUNK]) for u in range(2)]
        wt = s.sb("wt", [P, 3, CHALF, C])
        parts = [s.sb(f"parts{u}", [P, PARTS, 4, CHUNK], BF16) for u in range(2)]
        rest = s.sb("rest", [P, 4, BANK])
        v_out = [s.sb(f"v_out{u}", [P, NH, ROWS, HD]) for u in range(2)]
        qk_ps = s.ps("qk_ps", [P, 4, BANK])
        v_ps = s.ps("v_ps", [P, 4, BANK])
        ln = LayerNorm(s, CONV_EPS)
        w_loaded = s.sem("w_loaded")
        x_loaded = [s.sem(f"x_loaded{u}") for u in range(2)]
        centred, xn_ready = s.sem("centred"), s.sem("xn_ready")
        qk_done, hi_ready, rest_ready, mid_ready, low_ready = (s.sem(n) for n in ("qk_done", "hi_ready", "rest_ready", "mid_ready", "low_ready"))
        v_done, v_read = s.sem("v_done"), s.sem("v_read")
        stored = [s.sem(f"stored{u}") for u in range(2)]
        v_stored = [s.sem(f"v_stored{u}") for u in range(2)]
        block = ctx.enter_context(nc.Block())
        x_in = d["x"].rearrange("n (a c) i w -> n c a (i w)", a=CHALF)

        @block.sync
        def _(sp):
            for m in range(3):
                sp.dma_start(wt[:, m], d["w_t"][m].rearrange("(a c) o -> c a o", a=CHALF)).then_inc(w_loaded, 16)
            sp.sem_inc(centred, 2)
            with sp.Fori(0, N) as n:
                with sp.Fori(0, H // ROWS // 2) as i:
                    for u in range(2):
                        k = n * (H // ROWS) + i * 2 + u
                        sp.wait_ge(centred, k + 1)
                        for a in range(CHALF):
                            sp.dma_start(x[u][:, a * ROWS:(a + 1) * ROWS, :].rearrange("c i w -> c (i w)"),
                                         x_in[bass.ds(n, 1), :, a, bass.ds((i * 2 + u) * CHUNK, CHUNK)].rearrange("n c x -> (n c) x")).then_inc(x_loaded[u], 16)

        @block.vector
        def _(dve):
            dve.sem_inc(rest_ready, 4)
            dve.sem_inc(low_ready, 4)
            dve.sem_inc(v_done, 8)

            def body(k, u, first, last):
                def normalise(part, m, v):
                    if part == 0:
                        dve.wait_ge(x_loaded[v], 16 * m + 32 - 16 * v)
                        ln.mean_of(dve, x[v][:, :, :], m)
                    if part == 1:
                        ln.centre(dve, x[v][:, :, :], m).then_inc(centred, 1)
                    if part == 2:
                        ln.variance(dve, m)
                    if part == 3:
                        dve.wait_ge(v_done, 4 * m + 4)
                        ln.scale(dve, xn[v][:, :, :].rearrange("c a (i w) -> c (a i) w", w=W), m).then_inc(xn_ready, 1)

                if first:
                    for part in range(4):
                        normalise(part, 0, 0)
                for j in range(TILES):
                    if not last and j in (0, 2, 4, 6):
                        normalise(j // 2, k + 1, 1 - u)
                    g = TILES * k + j
                    dve.wait_ge(hi_ready, g + 1)
                    dve.wait_ge(low_ready, g + 1)
                    at = (j // 4) * BANK
                    dve.tensor_tensor(rest[:, j % 4], qk_ps[:, j % 4], parts[u][:, 0, j % 4, at:at + BANK], ALU.subtract).then_inc(rest_ready, 1)

            pipelined(dve, NCHUNK, body)

        @block.scalar
        def _(act):
            act.sem_inc(v_read, 4)
            for u in range(2):
                act.sem_inc(stored[u], 16 * PARTS)
                act.sem_inc(v_stored[u], 16)

            def body(k, u, first, last):
                def middle(j):
                    at = (j // 4) * BANK
                    act.wait_ge(rest_ready, TILES * k + j + 5)
                    act.activation(parts[u][:, 1, j % 4, at:at + BANK], rest[:, j % 4], ACT.Copy).then_inc(mid_ready, 1)

                def value(b):
                    act.wait_ge(v_done, 4 * k + b + 9)
                    if b == 0:
                        act.wait_ge(v_stored[u], 8 * k - 8 * u + 16)
                    act.activation(v_out[u][:, :, 2 * b:2 * b + 2, :].rearrange("w h i c -> w i h c"),
                                   v_ps[:, b].rearrange("w (i h c) -> w i h c", i=2, h=NH), ACT.Copy).then_inc(v_read, 1)

                def store(m, v):
                    act.wait_ge(low_ready, TILES * m + TILES + 4)
                    for p in range(PARTS):
                        act.dma_start(d["qk_parts"][p, :, :, bass.ds(m * CHUNK, CHUNK)].rearrange("t o x -> o t x"), parts[v][:, p]).then_inc(stored[v], 16)
                    act.wait_ge(v_read, 4 * m + 8)
                    act.dma_start(d["v_t"][bass.ds(m, 1)].rearrange("k h w x -> (k w) h x"),
                                  v_out[v][:, :, :, :].rearrange("w h i c -> w h (i c)")).then_inc(v_stored[v], 16)

                if first:
                    ln.square(act, centred, 3)
                    ln.root(act, 0)
                act.wait_ge(stored[u], 24 * k - 24 * u + 48)
                for j in range(TILES):
                    act.wait_ge(qk_done, TILES * k + j + 1)
                    at = (j // 4) * BANK
                    act.activation(parts[u][:, 0, j % 4, at:at + BANK], qk_ps[:, j % 4], ACT.Copy).then_inc(hi_ready, 1)
                    if j:
                        middle(j - 1)
                    if j == 1 and not first:
                        store(k - 1, 1 - u)
                    if j == 2 and not last:
                        ln.square(act, centred, k + 4)
                    if j == 5 and not last:
                        ln.root(act, k + 1)
                    if j == 4:
                        value(0)
                        value(1)
                middle(TILES - 1)
                value(2)
                value(3)
                if last:
                    store(k, u)

            pipelined(act, NCHUNK, body)
            for u in range(2):
                act.wait_ge(stored[u], 16 * PARTS * (NCHUNK // 2 + 1))
                act.wait_ge(v_stored[u], 16 * (NCHUNK // 2 + 1))

        @block.gpsimd
        def _(pool):
            with pool.Fori(0, NCHUNK // 2) as i:
                for u in range(2):
                    for j in range(TILES):
                        pool.wait_ge(mid_ready, TILES * (2 * i + u) + j + 1)
                        at = (j // 4) * BANK
                        pool.tensor_tensor(parts[u][:, 2, j % 4, at:at + BANK], rest[:, j % 4], parts[u][:, 1, j % 4, at:at + BANK],
                                           ALU.subtract).then_inc(low_ready, 1)

        @block.tensor
        def _(pe):
            pe.wait_ge(w_loaded, 48)
            with pe.Fori(0, NCHUNK // 2) as i:
                for u in range(2):
                    k = 2 * i + u
                    pe.wait_ge(xn_ready, k + 1)
                    for sub in range(2):
                        for j in range(4):
                            pe.wait_ge(rest_ready, TILES * k + 4 * sub + j + 1)
                            m, o = j // 2, j % 2
                            for a in range(CHALF):
                                last = pe.matmul(qk_ps[:, j], wt[:, m, a, o * P:(o + 1) * P], xn[u][:, a, sub * BANK:(sub + 1) * BANK],
                                                 start=a == 0, stop=a == CHALF - 1)
                            last.then_inc(qk_done, 1)
                        for b in (2 * sub, 2 * sub + 1):
                            pe.wait_ge(v_read, 4 * k + b + 1)
                            for r in range(2):
                                row = 2 * b + r
                                for a in range(CHALF):
                                    last = pe.matmul(v_ps[:, b, r * C:(r + 1) * C], xn[u][:, a, row * W:(row + 1) * W], wt[:, 2, a, :],
                                                     start=a == 0, stop=a == CHALF - 1)
                            last.then_inc(v_done, 1)


IHALF = H // 2
UNITS = NH * N * 2
QUADS = 4
JQ = W // QUADS
FIRST_PARTS = ((0, 3, (0, 0, 0)), (3, 2, (1, 1)), (5, 1, (2,)))
SECOND_PARTS = ((0, 3, (0, 1, 2)), (3, 2, (0, 1)), (5, 1, (0,)))
KROWS = PAIRS * HD


def attend(nc, d):
    with ExitStack() as ctx:
        s = Scope(nc, ctx, "att")
        PIECES, PR = 8, IHALF // 8
        RJ = W // 8
        FILL = 2 * BANK
        rs = [s.sb(f"rs{t}", [KROWS, W, W], BF16) for t in range(2)]
        rv = s.sb("rv", [P, W, HD])
        qa, ka, kb = (s.sb(n, [KROWS, IHALF, W], BF16) for n in ("qa", "ka", "kb"))
        scores = [s.sb(f"scores{v}", [P, IHALF, W]) for v in range(2)]
        vt = [s.sb(f"vt{f}", [P, IHALF, HD]) for f in range(2)]
        att_v = [s.sb(f"att_v{b}", [P, BANK]) for b in range(2)]
        att_r = s.sb("att_r", [P, IHALF, JQ])
        negmax, total, inverse = ([s.sb(f"{n}{v}", [P, IHALF]) for v in range(2)] for n in ("negmax", "total", "inverse"))
        sc_ps = s.ps("sc_ps", [P, 2, FILL])
        out_ps = s.ps("out_ps", [P, 4, BANK])
        rs_loaded = [s.sem(f"rs_loaded{q}") for q in range(4)]
        rv_loaded, qa_loaded, ka_loaded, kb_loaded = (s.sem(n) for n in ("rv_loaded", "qa_loaded", "ka_loaded", "kb_loaded"))
        v_loaded = [s.sem(f"v_loaded{f}") for f in range(2)]
        cleared, unit_begun = s.sem("cleared"), s.sem("unit_begun")
        rel_done, own_done, rel_read, added = (s.sem(n) for n in ("rel_done", "own_done", "rel_read", "added"))
        maxed, exped, summed, inverted, normed = (s.sem(n) for n in ("maxed", "exped", "summed", "inverted", "normed"))
        v_done, r_done, v_read, r_read = (s.sem(n) for n in ("v_done", "r_done", "v_read", "r_read"))
        v_stored = [s.sem(f"v_stored{b}") for b in range(2)]
        r_stored = s.sem("r_stored")
        block = ctx.enter_context(nc.Block())

        def steps(eng, step):
            step(0, 0, True, False, False)
            step(1, 1, True, True, False)
            with eng.Fori(1, UNITS // 2) as i:
                for v in range(2):
                    step(2 * i + v, v, True, True)
            step(UNITS, 0, False, True)

        def later(eng, semaphore, value):
            if not (isinstance(value, int) and value <= 0):
                eng.wait_ge(semaphore, value)

        @block.sync
        def _(sp):
            parts = d["qk_parts"].rearrange("p (m a) o x -> p m (a o) x", m=2)

            def load_stack(dst, groups, m, h, pixel, done):
                for g, n, which in groups:
                    src = parts[which[0]:which[-1] + 1, m, bass.ds(h * HD, HD), bass.ds(pixel, 8 * CHUNK)].rearrange("p c x -> c p x")
                    if len(set(which)) < n:
                        src = src.broadcast_to([HD, n, 8 * CHUNK])
                    sp.dma_start(dst[g * HD:(g + n) * HD, :, :].rearrange("r i w -> r (i w)"), src).then_inc(done, 16)

            def load_relative(h, q, need):
                later(sp, rel_done, need)
                sp.sem_inc(unit_begun, 1)
                for t in range(2):
                    for g, n, which in SECOND_PARTS:
                        sp.dma_start(rs[t][g * HD:(g + n) * HD, q * JQ:(q + 1) * JQ, :].rearrange("r j w -> r (j w)"),
                                     d["r_parts"][t, which[0]:which[-1] + 1, :, bass.ds(h, 1), q * JQ * W:(q + 1) * JQ * W].rearrange("p c h x -> (c h) p x")).then_inc(rs_loaded[q], 16)

            def unit(h, n, f, first_of_head, u):
                pixel, k = n * PIX + f * (PIX // 2), n * (H // ROWS) + f * 8
                if first_of_head:
                    for q in range(4):
                        load_relative(h, q, 8 * u - 6 + 2 * q)
                later(sp, rel_done, 8 * u)
                load_stack(ka, FIRST_PARTS, 1, h, pixel, ka_loaded)
                later(sp, own_done, 8 * u)
                sp.sem_inc(unit_begun, 1)
                load_stack(qa, FIRST_PARTS, 0, h, pixel, qa_loaded)
                load_stack(kb, SECOND_PARTS, 1, h, pixel, kb_loaded)
                later(sp, v_done, 4 * (u - 1))
                sp.sem_inc(unit_begun, 1)
                sp.dma_start(vt[f][:, :, :].rearrange("w i c -> w (i c)"),
                             d["v_t"][bass.ds(k, 8), bass.ds(h, 1)].rearrange("k h w x -> (h w) k x")).then_inc(v_loaded[f], 16)

            def head(h, u):
                for n in range(1):
                    unit(h, 0, 0, True, u)
                    unit(h, 0, 1, False, u + 1)
                    later(sp, r_done, 4 * u)
                    sp.dma_start(rv[:, :, :].rearrange("w j c -> w (j c)"), d["rv_t"][bass.ds(h, 1)].rearrange("h w x -> (h w) x")).then_inc(rv_loaded, 16)
                with sp.Fori(1, N) as n:
                    for f in range(2):
                        unit(h, n, f, False, u + 2 * n + f)

            head(0, 0)
            with sp.Fori(1, NH) as h:
                head(h, 8 * h)

        @block.tensor
        def _(pe):
            pe.wait_ge(cleared, 1)

            def own_scores(u, p):
                if p == 0:
                    pe.wait_ge(kb_loaded, 48 * u + 48)
                if p < 2:
                    pe.wait_ge(rel_read, 8 * u + 7 + p)
                else:
                    pe.wait_ge(added, 8 * u + p - 1)
                for r in range(PR):
                    i = p * PR + r
                    last = pe.matmul(sc_ps[:, p % 2, r * W:(r + 1) * W], kb[:, i, :], qa[:, i, :], start=True, stop=True)
                last.then_inc(own_done, 1)

            def sums_with_v(u, v, p):
                b = p // 2
                if p == 0:
                    pe.wait_ge(v_loaded[1 - v], 8 * (u - 1) - 8 * (1 - v) + 16)
                if p % 2 == 0:
                    later(pe, r_read, 4 * (u - 2) + b + 1)
                pe.wait_ge(normed, 8 * (u - 1) + p + 1)
                for g2 in range(2):
                    for r in range(4):
                        for g1 in range(1):
                            i = p * PR + g2 * 4 + r
                            g = (p % 2) * 2 + g2
                            last = pe.matmul(out_ps[32 * g:32 * g + HD, b, r * W:(r + 1) * W], vt[1 - v][:, i, :], scores[1 - v][:, i, :],
                                             start=True, stop=True, tile_position=(0, 32 * g))
                if p % 2 == 1:
                    last.then_inc(v_done, 1)

            def step(u, v, now, before, second=True):
                if now:
                    pe.wait_ge(ka_loaded, 48 * u + 48)
                    pe.wait_ge(qa_loaded, 48 * u + 48)
                    for r in range(8):
                        if r % 2 == 0:
                            pe.wait_ge(rs_loaded[r // 2], (u // 8) * 96 + 96)
                        if r < 2:
                            later(pe, added, 8 * u + r - 1)
                        else:
                            pe.wait_ge(rel_read, 8 * u + r - 1)
                        for jj in range(RJ):
                            j = r * RJ + jj
                            for t, moving in ((0, qa), (1, ka)):
                                last = pe.matmul(sc_ps[:, r % 2, jj * IHALF:(jj + 1) * IHALF], rs[t][:, j, :], moving[:, :, j],
                                                 start=t == 0, stop=t == 1)
                        last.then_inc(rel_done, 1)
                for p in range(PIECES + 1):
                    if now and p < PIECES:
                        own_scores(u, p)
                    if before and p > 0:
                        sums_with_v(u, v, p - 1)
                if before:
                    pe.wait_ge(rv_loaded, ((u - 1) // 8) * 16 + 16)
                    for b in range(4):
                        pe.wait_ge(v_read, 4 * (u - 1) + b + 1)
                        for jj in range(8):
                            for g in range(QUADS):
                                j = g * JQ + b * 8 + jj
                                last = pe.matmul(out_ps[32 * g:32 * g + HD, b, jj * IHALF:(jj + 1) * IHALF], rv[:, j, :], scores[1 - v][:, :, j],
                                                 start=True, stop=True, tile_position=(0, 32 * g))
                        last.then_inc(r_done, 1)

            steps(pe, step)

        @block.scalar
        def _(act):
            def exp_piece(u, v, p):
                act.wait_ge(maxed, 8 * u + p + 1)
                for r in range(PR):
                    i = p * PR + r
                    last = act.activation(scores[v][:, i, :], scores[v][:, i, :], ACT.Exp, bias=negmax[v][:, i:i + 1])
                last.then_inc(exped, 1)

            act.sem_inc(r_stored, 64)
            LATE_AFTER = (1,)
            STORE_AFTER = (1, 2, 4, 5)

            def store_v(u, b):
                act.wait_ge(v_read, 4 * u + b + 1)
                for g in range(QUADS):
                    at = (16 * b + 4 * g) * W
                    act.dma_start(d["att_v"][bass.ds(u % 8, 1), bass.ds((u // 8) * HD, HD), at:at + BANK].rearrange("u c x -> (u c) x"),
                                  att_v[b % 2][32 * g:32 * g + HD, :]).then_inc(v_stored[b % 2], 16)

            def read_r(u, b):
                act.wait_ge(r_done, 4 * u + b + 1)
                if b == 0:
                    act.wait_ge(r_stored, 64 * u + 64)
                act.activation(att_r[:, :, 8 * b:8 * b + 8], out_ps[:, b, :].rearrange("p (j i) -> p i j", j=8), ACT.Copy).then_inc(r_read, 1)

            def store_r(u):
                act.wait_ge(r_read, 4 * u + 4)
                for g in range(QUADS):
                    act.dma_start(d["att_r"][bass.ds(u % 8, 1), bass.ds((u // 8) * HD, HD), g].rearrange("u c i j -> (u c) i j"), att_r[32 * g:32 * g + HD, :, :]).then_inc(r_stored, 16)

            def step(u, v, now, before, second=True):
                for r in range(8):
                    if now:
                        act.wait_ge(rel_done, 8 * u + r + 1)
                        if r == 0:
                            later(act, r_done, 4 * (u - 1))
                        act.activation(scores[v][:, :, r * RJ:(r + 1) * RJ], sc_ps[:, r % 2, :].rearrange("w (j i) -> w i j", i=IHALF), ACT.Copy).then_inc(rel_read, 1)
                    if before and r in LATE_AFTER:
                        exp_piece(u - 1, 1 - v, PIECES - len(LATE_AFTER) + LATE_AFTER.index(r))
                    if second and r % 2 == 1:
                        read_r(u - 2, r // 2)
                if second:
                    store_r(u - 2)
                for p in range(PIECES - len(LATE_AFTER)):
                    if now:
                        exp_piece(u, v, p)
                    if before and p in STORE_AFTER:
                        store_v(u - 1, STORE_AFTER.index(p))

            steps(act, step)
            for b in range(4):
                read_r(UNITS - 1, b)
            store_r(UNITS - 1)
            act.wait_ge(r_stored, 64 * UNITS + 64)
            for b in range(2):
                act.wait_ge(v_stored[b], 128 * UNITS)

        @block.vector
        def _(dve):
            dve.memset(out_ps[:, :, :], 0.0).then_inc(cleared, 1)

            def sums(u, v, p):
                rows = slice(p * PR, (p + 1) * PR)
                dve.wait_ge(exped, 8 * u + p + 1)
                dve.tensor_reduce(total[v][:, rows], scores[v][:, rows, :], AX_X, ALU.add).then_inc(summed, 1)
                dve.wait_ge(summed, 8 * u + p + 1)
                dve.reciprocal(inverse[v][:, rows], total[v][:, rows]).then_inc(inverted, 1)

            def read_v(u, b):
                dve.wait_ge(v_done, 4 * u + b + 1)
                later(dve, v_stored[b % 2], 64 * (2 * u + b // 2))
                dve.tensor_copy(att_v[b % 2][:, :], out_ps[:, b, :]).then_inc(v_read, 1)

            def add(u, v, p):
                rows = slice(p * PR, (p + 1) * PR)
                dve.wait_ge(own_done, 8 * u + p + 1)
                if p == 0:
                    dve.wait_ge(rel_read, 8 * u + 8)
                dve.tensor_tensor(scores[v][:, rows, :], sc_ps[:, p % 2, :].rearrange("w (i j) -> w i j", j=W), scores[v][:, rows, :], ALU.add).then_inc(added, 1)

            def largest(u, v, p):
                rows = slice(p * PR, (p + 1) * PR)
                dve.wait_ge(added, 8 * u + p + 1)
                dve.tensor_reduce(negmax[v][:, rows], scores[v][:, rows, :], AX_X, ALU.max, negate=True).then_inc(maxed, 1)

            ORDER = (("add", 0), ("max", 0), ("add", 1), ("max", 1), ("add", 2), ("add", 3), ("v", 0), ("max", 2), ("add", 4), ("add", 5), ("v", 1),
                     ("max", 3), ("add", 6), ("add", 7), ("v", 2), ("max", 4), ("v", 3), ("max", 5), ("sum", 0), ("max", 6), ("sum", 1), ("max", 7),
                     ("sum", 2), ("sum", 3), ("sum", 4), ("sum", 5), ("sum", 6), ("sum", 7))

            def step(u, v, now, before, second=True):
                for what, p in ORDER:
                    if what == "v":
                        if before:
                            read_v(u - 1, p)
                    elif now:
                        {"add": add, "max": largest, "sum": sums}[what](u, v, p)

            steps(dve, step)

        @block.gpsimd
        def _(pool):
            def normalise(u, v, p):
                rows = slice(p * PR, (p + 1) * PR)
                pool.wait_ge(inverted, 8 * u + p + 1)
                pool.tensor_tensor(scores[v][:, rows, :], scores[v][:, rows, :], inverse[v][:, rows].unsqueeze(2).broadcast_to([P, PR, W]),
                                   ALU.mult).then_inc(normed, 1)

            with pool.Fori(0, UNITS // 2) as i:
                for v in range(2):
                    for p in range(PIECES):
                        normalise(2 * i + v, v, p)


def combine(nc, d):
    with ExitStack() as ctx:
        s = Scope(nc, ctx, "comb")
        PER = H // ROWS
        sum_v = [s.sb(f"sum_v{u}", [P, CHALF, CHUNK]) for u in range(2)]
        sum_r = [s.sb(f"sum_r{u}", [P, CHALF, QUADS, ROWS, JQ]) for u in range(2)]
        x = [s.sb(f"x{u}", [P, CHALF, CHUNK]) for u in range(2)]
        att = [s.sb(f"att{u}", [P, CHALF, CHUNK]) for u in range(2)]
        x1 = [s.sb(f"x1{u}", [P, CHALF, CHUNK]) for u in range(2)]
        tn = [s.sb(f"tn{u}", [P, GROUPS, W]) for u in range(2)]
        tnt = s.sb("tnt", [P, 4, BANK])
        logits = s.sb("logits", [P, P, H])
        wo = s.sb("wo", [P, CHALF, C])
        gate = s.sb("gate", [EXPERTS, W])
        gate_t = s.sb("gate_t", [P, EXPERTS])
        gate_b = s.sb("gate_b", [P, 1])
        ident = s.sb("ident", [P, P])
        top = s.sb("top", [P, TOPK])
        top_at = s.sb("top_at", [P, TOPK], U32)
        neg = s.sb("neg", [P, 1])
        expsum = s.sb("expsum", [P, 1])
        y_ps = s.ps("y_ps", [P, 4, BANK])
        t_ps = s.ps("t_ps", [P, 2, BANK])
        l_ps = s.ps("l_ps", [P, 2, BANK])
        ln = LayerNorm(s, TOKEN_EPS)
        consts_loaded, ident_zero, ident_ready, gate_turned, gate_ready = (s.sem(n) for n in ("consts_loaded", "ident_zero", "ident_ready", "gate_turned", "gate_ready"))
        loaded = [s.sem(f"loaded{u}") for u in range(2)]
        att_ready, y_done, x1_ready, centred, tn_ready = (s.sem(n) for n in ("att_ready", "y_done", "x1_ready", "centred", "tn_ready"))
        turned, tnt_ready, l_done, l_ready = (s.sem(n) for n in ("turned", "tnt_ready", "l_done", "l_ready"))
        x1_stored = [s.sem(f"x1_stored{u}") for u in range(2)]
        cleared, topped, found, negated, summed, cand_stored = (s.sem(n) for n in ("cleared", "topped", "found", "negated", "summed", "cand_stored"))
        block = ctx.enter_context(nc.Block())
        x_in, x1_out = (d[n].rearrange("n (a c) i w -> n c a (i w)", a=CHALF) for n in ("x", "out"))
        DMAS = 2 + 2 + 2

        def images(eng, body, after=None):
            with eng.Fori(0, N) as n:
                body(n * PER, 0, 0)
                body(n * PER + 1, 1, 1)
                with eng.Fori(1, PER // 2 - 1) as i:
                    for u in range(2):
                        body(n * PER + 2 * i + u, u, 2)
                body(n * PER + PER - 2, 0, PER - 2)
                body(n * PER + PER - 1, 1, PER - 1)
                if after:
                    after(n)

        @block.sync
        def _(sp):
            sp.dma_start(wo[:, :, :], d["w_t"][3].rearrange("(a c) o -> c a o", a=CHALF)).then_inc(consts_loaded, 16)
            sp.dma_start(gate[:, :], d["gate_w"]).then_inc(consts_loaded, 16)
            for a in range(CHALF):
                sp.dma_start(gate_b[a * EXPERTS:(a + 1) * EXPERTS, :], d["gate_b"].rearrange("(e z) -> e z", z=1)).then_inc(consts_loaded, 16)
            with sp.Fori(0, N) as n:
                for f in range(2):
                    with sp.Fori(0, PER // 4) as i:
                        for u in range(2):
                            at = 2 * i + u
                            k = n * PER + f * (PER // 2) + at
                            sp.wait_ge(att_ready, 2 * k + 2)
                            for a in range(CHALF):
                                sp.dma_start(sum_v[u][:, a, :], d["att_v"].rearrange("(n f) (a c) x -> n f a c x", f=2, a=CHALF)[bass.ds(n, 1), f, a, :, bass.ds(at * CHUNK, CHUNK)]
                                             .rearrange("n c x -> (n c) x")).then_inc(loaded[u], 16)
                                sp.dma_start(sum_r[u][:, a].rearrange("c g i j -> c g (i j)"),
                                             d["att_r"].rearrange("(n f) (a c) g i j -> n f a c g (i j)", f=2, a=CHALF)[bass.ds(n, 1), f, a, :, :, bass.ds(at * ROWS * JQ, ROWS * JQ)]
                                             .rearrange("n c g x -> (n c) g x")).then_inc(loaded[u], 16)
                            sp.wait_ge(x1_ready, 4 * k + 4)
                            for a in range(CHALF):
                                sp.dma_start(x[u][:, a, :], x_in[bass.ds(n, 1), :, a, bass.ds((f * (PER // 2) + at) * CHUNK, CHUNK)]
                                             .rearrange("n c x -> (n c) x")).then_inc(loaded[u], 16)

        @block.gpsimd
        def _(pool):
            make_identity(pool, ident, ident_zero, ident_ready)
            pool.sem_inc(att_ready, 4)
            with pool.Fori(0, N * PER // 2) as i:
                for u in range(2):
                    k = 2 * i + u
                    pool.wait_ge(loaded[u], i * 16 * DMAS + 16 * DMAS)
                    pool.wait_ge(y_done, 4 * k + 4)
                    for a in range(CHALF):
                        pool.tensor_tensor(att[u][:, a, :].rearrange("c (i g j) -> c i g j", i=ROWS, g=QUADS),
                                           sum_v[u][:, a, :].rearrange("c (i g j) -> c i g j", i=ROWS, g=QUADS),
                                           sum_r[u][:, a].rearrange("c g i j -> c i g j"), ALU.add).then_inc(att_ready, 1)

        @block.tensor
        def _(pe):
            pe.sem_inc(y_done, 8)
            pe.wait_ge(ident_ready, 1)
            pe.wait_ge(consts_loaded, 64)
            pe.transpose(t_ps[:, 0, 0:EXPERTS], gate[:, :], ident[0:EXPERTS, 0:EXPERTS]).then_inc(gate_turned, 1)
            pe.wait_ge(gate_ready, 1)

            def project_out(k, u):
                pe.wait_ge(att_ready, 2 * k + 6)
                for b in range(4):
                    sub, o = b // 2, b % 2
                    pe.wait_ge(x1_ready, 4 * k + b + 5)
                    for a in range(CHALF):
                        last = pe.matmul(y_ps[:, b], wo[:, a, o * P:(o + 1) * P], att[u][:, a, sub * BANK:(sub + 1) * BANK],
                                         start=a == 0, stop=a == CHALF - 1)
                    last.then_inc(y_done, 1)

            def body(k, u, place):
                if place == 0:
                    project_out(k, 0)
                    project_out(k + 1, 1)
                if place < PER - 2:
                    project_out(k + 2, u)
                pe.wait_ge(tn_ready, k + 1)
                for q in range(4):
                    pe.wait_ge(tnt_ready, 4 * k + q + 1)
                    a, rows = q // 2, range(4 * (q % 2), 4 * (q % 2) + 4)
                    for r, i in enumerate(rows):
                        last = pe.transpose(t_ps[:, q % 2, r * P:(r + 1) * P], tn[u][:, a * ROWS + i, :], ident[:, :])
                    last.then_inc(turned, 1)
                pe.wait_ge(tnt_ready, 4 * k + 6)
                for sub in range(2):
                    pe.wait_ge(l_ready, 2 * k + sub + 1)
                    for a in range(CHALF):
                        last = pe.matmul(l_ps[a * EXPERTS:(a + 1) * EXPERTS, sub], gate_t[:, :], tnt[:, 2 * a + sub, :], start=True, stop=True,
                                         tile_position=(0, a * EXPERTS))
                    last.then_inc(l_done, 1)

            images(pe, body)

        @block.vector
        def _(dve):
            dve.sem_inc(x1_ready, 8)
            dve.wait_ge(gate_turned, 1)
            dve.tensor_copy(gate_t[:, :], t_ps[:, 0, 0:EXPERTS]).then_inc(gate_ready, 1)

            def residual(k, u, half_k):
                for b in range(4):
                    sub, o = b // 2, b % 2
                    dve.wait_ge(y_done, 4 * k + b + 9)
                    if b == 0:
                        dve.wait_ge(loaded[u], 8 * DMAS * k - 8 * DMAS * u + 16 * DMAS)
                        dve.wait_ge(x1_stored[u], 16 * k - 16 * u + 32)
                    at = slice(sub * BANK, (sub + 1) * BANK)
                    dve.tensor_tensor(x1[u][:, o, at], y_ps[:, b], x[u][:, o, at], ALU.add).then_inc(x1_ready, 1)

            def body(k, u, place):
                if place == 0:
                    residual(k, 0, 0)
                dve.wait_ge(x1_ready, 4 * k + 12)
                rows = x1[u][:, :, :].rearrange("c a (i w) -> c (a i) w", w=W)
                ln.mean_of(dve, rows, k)
                ln.centre(dve, rows, k).then_inc(centred, 1)
                if place < PER - 1:
                    residual(k + 1, 1 - u, 0)
                ln.variance(dve, k)
                dve.wait_ge(turned, 4 * k + 4)
                ln.scale(dve, tn[u][:, :, :], k).then_inc(tn_ready, 1)

            def best(n):
                dve.wait_ge(l_ready, 2 * PER * n + 2 * PER + 2)
                dve.wait_ge(cand_stored, 48 * n + 48)
                dve.memset(neg[:, :], 0.0).then_inc(cleared, 1)
                every = logits[:, :, :].rearrange("p c i -> p (c i)")
                dve.max(top[:, :], every).then_inc(topped, 1)
                dve.wait_ge(cleared, n + 1)
                dve.wait_ge(topped, n + 1)
                dve.tensor_scalar(neg[:, :], top[:, 0:1], -1.0, None, ALU.mult).then_inc(negated, 1)
                dve.max_index(top_at[:, :], top[:, :], every).then_inc(found, 1)

            images(dve, body, best)

        @block.scalar
        def _(act):
            act.sem_inc(turned, 8)
            act.sem_inc(tnt_ready, 2)
            act.sem_inc(l_ready, 2)
            act.sem_inc(cand_stored, 48)
            for u in range(2):
                act.sem_inc(x1_stored[u], 32)
            act.wait_ge(consts_loaded, 64)

            def keep(k):
                for sub in range(2):
                    act.wait_ge(l_done, 2 * k + sub + 3)
                    row = (k % PER) * ROWS + 4 * sub
                    act.activation(logits[:, :, bass.ds(row, 4)].rearrange("p c i -> p i c"), l_ps[:, sub].rearrange("p (i c) -> p i c", i=4),
                                   ACT.Identity, bias=gate_b[:, :]).then_inc(l_ready, 1)

            def body(k, u, place):
                ln.square(act, centred, k + 1)
                if place:
                    keep(k - 1)
                ln.root(act, k)
                for a in range(CHALF):
                    act.dma_start(x1_out[bass.ds(k // PER, 1), :, a, bass.ds((k % PER) * CHUNK, CHUNK)].rearrange("n c x -> (n c) x"),
                                  x1[u][:, a, :]).then_inc(x1_stored[u], 16)
                for q in range(4):
                    act.wait_ge(turned, 4 * k + q + 9)
                    if q == 0:
                        act.wait_ge(l_done, 2 * k + 2)
                    act.activation(tnt[:, q], t_ps[:, q % 2], ACT.Copy).then_inc(tnt_ready, 1)
                if place == PER - 1:
                    keep(k)

            def exponentials(n):
                act.wait_ge(negated, n + 1)
                act.wait_ge(found, n + 1)
                every = logits[:, :, :].rearrange("p c i -> p (c i)")
                act.activation(every, every, ACT.Exp, bias=neg[:, :], accum_out=expsum[:, :]).then_inc(summed, 1)
                act.wait_ge(summed, n + 1)
                for name, tile in (("cand", top), ("cand_at", top_at), ("cand_sum", expsum)):
                    act.dma_start(d[name][bass.ds(n, 1)].rearrange("n p k -> (n p) k"), tile[:, :]).then_inc(cand_stored, 16)

            act.sem_inc(l_done, 2)
            images(act, body, exponentials)
            act.wait_ge(cand_stored, 48 * N + 48)
            for u in range(2):
                act.wait_ge(x1_stored[u], 32 * (N * PER // 2 + 1))


SLOTS = N * TOPK // 2
COLS = TOPK // 2
TOKENS = N * C * H
SKIP = 2 * TOKENS


def experts(nc, d):
    with ExitStack() as ctx:
        s = Scope(nc, ctx, "exp")
        GE = 8
        HC = HID // P
        cand = s.sb("cand", [EXPERTS, N, 2 * TOPK])
        cand_at = s.sb("cand_at", [EXPERTS, N, 2 * TOPK], U32)
        cand_sum = s.sb("cand_sum", [EXPERTS, N, 2])
        cand_tok = s.sb("cand_tok", [EXPERTS, N, 2 * TOPK])
        order = s.sb("order", [EXPERTS, 2 * TOPK])
        best = s.sb("best", [EXPERTS, N, TOPK])
        best_at = s.sb("best_at", [EXPERTS, N, TOPK], U32)
        best_pos = s.sb("best_pos", [EXPERTS, N, TOPK])
        same = s.sb("same", [EXPERTS, N, TOPK, 2 * TOPK])
        token = s.sb("token", [EXPERTS, N, TOPK])
        off = s.sb("off", [EXPERTS, N, 2 + TOPK])
        expo = s.sb("expo", [EXPERTS, N, 2 + TOPK])
        z = s.sb("z", [EXPERTS, N, 2])
        zsum, zinv = s.sb("zsum", [EXPERTS, N]), s.sb("zinv", [EXPERTS, N])
        prob = s.sb("prob", [EXPERTS, N, TOPK])
        weight = s.sb("weight", [P, SLOTS])
        index = s.sb("index", [P, SLOTS])
        index_u = s.sb("index_u", [P, SLOTS], U32)
        dup, index_w, index_wu = s.sb("dup", [P, SLOTS]), s.sb("index_w", [P, SLOTS]), s.sb("index_wu", [P, SLOTS], U32)
        rows = s.sb("rows", [P, SLOTS, W])
        tn = s.sb("tn", [P, SLOTS, W])
        weighted = s.sb("weighted", [P, SLOTS, W])
        result = s.sb("result", [P, SLOTS, W])
        ident = s.sb("ident", [P, P])
        fold = s.sb("fold", [P, EXPERTS])
        earlier = s.sb("earlier", [P, COLS, COLS * P])
        spread = s.sb("spread", [P, SLOTS, P])
        index_row = s.sb("index_row", [P, SLOTS, P])
        equal = s.sb("equal", [P, SLOTS, COLS * P])
        first_only = s.sb("first_only", [P, COLS, COLS * P])
        pooled = s.sb("pooled", [P, EXPERTS, N])
        pooled_g = [s.sb(f"pooled_g{u}", [P, GE, N]) for u in range(2)]
        b1, b2 = s.sb("b1", [EXPERTS, HID]), s.sb("b2", [EXPERTS, W])
        b1_t, b2_t = s.sb("b1_t", [P, EXPERTS, HC]), s.sb("b2_t", [P, EXPERTS])
        w1 = [s.sb(f"w1{u}", [P, GE, HID]) for u in range(2)]
        w2 = [s.sb(f"w2{u}", [P, GE, HC * W]) for u in range(2)]
        hid_in = [s.sb(f"hid_in{u}", [P, GE * HC, N]) for u in range(2)]
        hid = [s.sb(f"hid{u}", [P, GE * HC, N]) for u in range(2)]
        out_t = s.sb("out_t", [P, N, 2, EXPERTS])
        a_ps = s.ps("a_ps", [P, 4, BANK])
        p_ps = s.ps("p_ps", [P, BANK])
        h_ps = [s.ps(f"h_ps{u}", [P, BANK]) for u in range(2)]
        o_ps = [s.ps("o_ps", [P, BANK]), p_ps]
        ln = LayerNorm(s, TOKEN_EPS)
        names = ("loaded", "tick", "ident_zero", "ident_ready", "consts", "offs", "expd", "indexed", "gathered", "centred", "scaled", "pooled_done", "pooled_ready",
                 "bias_turned", "bias_ready", "spread_ready", "index_turned", "index_copied", "group_ready", "hid_done", "hid_biased",
                 "hid_ready", "out_done", "out_ready", "out_turned", "weighted_ready", "equal_ready", "summed", "result_ready", "scattered")
        m = {n: s.sem(n) for n in names}
        w_loaded = [s.sem(f"w_loaded{u}") for u in range(2)]
        block = ctx.enter_context(nc.Block())
        table = d["out"].rearrange("n c i w -> (n c i) w")

        @block.sync
        def _(sp):
            for a in range(2):
                at = slice(a * TOPK, (a + 1) * TOPK)
                half = slice(a * EXPERTS, (a + 1) * EXPERTS)
                sp.dma_start(cand[:, :, at], d["cand"][:, half, :].rearrange("n e k -> e n k")).then_inc(m["loaded"], 16)
                sp.dma_start(cand_at[:, :, at], d["cand_at"][:, half, :].rearrange("n e k -> e n k")).then_inc(m["loaded"], 16)
                sp.dma_start(cand_sum[:, :, a:a + 1], d["cand_sum"][:, half, :].rearrange("n e k -> e n k"), allow_slow_non_contiguous=True).then_inc(m["loaded"], 16)
            sp.dma_start(b1[:, :], d["weight1"][:, W, :]).then_inc(m["loaded"], 16)
            sp.dma_start(b2[:, :], d["weight2"][:, HID, :]).then_inc(m["loaded"], 16)
            sp.sem_inc(m["out_done"], 2)
            with sp.Fori(0, EXPERTS // GE // 2) as i:
                for u in range(2):
                    sp.wait_ge(m["out_done"], 2 * i + u + 1)
                    sp.dma_start(w1[u][:, :, :], d["weight1"][bass.ds((2 * i + u) * GE, GE), 0:W, :].rearrange("e x h -> x e h")).then_inc(w_loaded[u], 16)
                    sp.dma_start(w2[u][:, :, :], d["weight2"][bass.ds((2 * i + u) * GE, GE), 0:HID, :].rearrange("e (p c) o -> p e (c o)", c=HC)).then_inc(w_loaded[u], 16)

        @block.gpsimd
        def _(pool):
            make_identity(pool, ident, m["ident_zero"], m["ident_ready"])
            pool.memset(fold[:, :], 0.0).then_inc(m["consts"], 1)
            pool.memset(earlier[:, :, :], 1.0).then_inc(m["consts"], 1)
            pool.iota(order[:, :], [[1, 2 * TOPK]], base=0, channel_multiplier=0, allow_small_or_imprecise_dtypes=True).then_inc(m["consts"], 1)
            pool.wait_ge(m["consts"], 3)
            for a in range(2):
                pool.affine_select(out=fold[:, :], in_=fold[:, :], compare_op=ALU.not_equal, fill=1.0, base=-a * EXPERTS,
                                   pattern=[[-1, EXPERTS]], channel_multiplier=1).then_inc(m["consts"], 1)
                pool.wait_ge(m["consts"], 4 + a)
            for q in range(COLS):
                pool.affine_select(out=earlier[:, q, :], in_=earlier[:, q, :], compare_op=ALU.is_gt, fill=0.0, base=q * P,
                                   pattern=[[-1, COLS * P]], channel_multiplier=1).then_inc(m["consts"], 1)
            pool.wait_ge(m["indexed"], 1)
            for c in range(SLOTS):
                pool.indirect_dma_start(out=rows[:, c, :], out_offset=None, in_=table,
                                        in_offset=bass.IndirectOffsetOnAxis(ap=index_u[:, c:c + 1], axis=0)).then_inc(m["gathered"], 16)
            for n in range(N):
                pool.wait_ge(m["result_ready"], n + 1)
                for c in range(n * COLS, (n + 1) * COLS):
                    pool.indirect_dma_start(out=table, out_offset=bass.IndirectOffsetOnAxis(ap=index_wu[:, c:c + 1], axis=0), in_=result[:, c, :],
                                            in_offset=None, bounds_check=TOKENS - 1, oob_is_err=False).then_inc(m["scattered"], 16)
            pool.wait_ge(m["scattered"], 16 * SLOTS)

        @block.vector
        def _(dve):
            ticks = [0]

            def done(instruction):
                ticks[0] += 1
                instruction.then_inc(m["tick"], 1)
                dve.wait_ge(m["tick"], ticks[0])

            dve.wait_ge(m["loaded"], 16 * 8)
            dve.wait_ge(m["consts"], 3)
            for n in range(N):
                done(dve.max(best[:, n, :], cand[:, n, :]))
                done(dve.max_index(best_at[:, n, :], best[:, n, :], cand[:, n, :]))
            for a in range(2):
                dve.tensor_tensor(off[:, :, a:a + 1], cand[:, :, a * TOPK:a * TOPK + 1], best[:, :, 0:1], ALU.subtract).then_inc(m["offs"], 1)
            dve.tensor_tensor(off[:, :, 2:], best[:, :, :], best[:, :, 0:1].broadcast_to([EXPERTS, N, TOPK]), ALU.subtract).then_inc(m["offs"], 1)
            done(dve.tensor_copy(cand_tok[:, :, :], cand_at[:, :, :]))
            for n in range(N):
                for a in range(2):
                    at = slice(a * TOPK, (a + 1) * TOPK)
                    done(dve.tensor_scalar(cand_tok[:, n, at], cand_tok[:, n, at], float((n * CHALF + a) * P * H), None, ALU.add))
            done(dve.tensor_copy(best_pos[:, :, :], best_at[:, :, :]))
            for n in range(N):
                shape = [EXPERTS, TOPK, 2 * TOPK]
                done(dve.tensor_tensor(same[:, n], best_pos[:, n, :].unsqueeze(2).broadcast_to(shape), order[:, :].unsqueeze(1).broadcast_to(shape), ALU.is_equal))
                done(dve.tensor_tensor(same[:, n], same[:, n], cand_tok[:, n, :].unsqueeze(1).broadcast_to(shape), ALU.mult))
            done(dve.tensor_reduce(token[:, :, :], same[:, :, :, :], AX_X, ALU.add))
            for k in range(2):
                done(dve.tensor_copy(index[k * EXPERTS:(k + 1) * EXPERTS, :], token[:, :, k::2].rearrange("e n q -> e (n q)")))
            dve.tensor_copy(index_u[:, :], index[:, :]).then_inc(m["indexed"], 1)
            dve.tensor_copy(spread[:, :, :], index[:, :].unsqueeze(2).broadcast_to([P, SLOTS, P])).then_inc(m["spread_ready"], 1)
            dve.wait_ge(m["expd"], 1)
            done(dve.tensor_tensor(z[:, :, :], expo[:, :, 0:2], cand_sum[:, :, :], ALU.mult))
            done(dve.tensor_reduce(zsum[:, :], z[:, :, :], AX_X, ALU.add))
            done(dve.reciprocal(zinv[:, :], zsum[:, :]))
            done(dve.tensor_tensor(prob[:, :, :], expo[:, :, 2:], zinv[:, :].unsqueeze(2).broadcast_to([EXPERTS, N, TOPK]), ALU.mult))
            for k in range(2):
                done(dve.tensor_copy(weight[k * EXPERTS:(k + 1) * EXPERTS, :], prob[:, :, k::2].rearrange("e n q -> e (n q)")))
            dve.wait_ge(m["bias_turned"], 1)
            for c in range(HC):
                done(dve.tensor_copy(b1_t[:, :, c], a_ps[:, 0, c * EXPERTS:(c + 1) * EXPERTS]))
            dve.tensor_copy(b2_t[:, :], a_ps[:, 0, HC * EXPERTS:(HC + 1) * EXPERTS]).then_inc(m["bias_ready"], 1)
            dve.wait_ge(m["gathered"], 16 * SLOTS)
            ln.mean_of(dve, rows[:, :, :], 0)
            ln.centre(dve, rows[:, :, :], 0).then_inc(m["centred"], 1)
            ln.variance(dve, 0)
            done(ln.scale(dve, tn[:, :, :], 0))
            dve.tensor_tensor(tn[:, :, :], tn[:, :, :], weight[:, :].unsqueeze(2).broadcast_to([P, SLOTS, W]), ALU.mult).then_inc(m["scaled"], 1)
            dve.wait_ge(m["pooled_done"], 1)
            done(dve.tensor_copy(pooled[:, :, :].rearrange("x e n -> x n e"), p_ps[:, 0:N * EXPERTS].rearrange("x (n e) -> x n e", n=N)))
            dve.wait_ge(m["bias_ready"], 1)

            def give(g, u):
                dve.wait_ge(m["hid_done"], g + 1)
                dve.tensor_copy(pooled_g[u][:, :, :], pooled[:, bass.ds(g * GE, GE), :]).then_inc(m["group_ready"], 1)

            def bias(g, u):
                dve.wait_ge(m["hid_done"], g + 3)
                dve.tensor_tensor(hid_in[u][:, :, :], h_ps[u][:, 0:GE * HC * N].rearrange("p (c n) -> p c n", n=N),
                                  b1_t[:, bass.ds(g * GE, GE), :].rearrange("p e c -> p (e c)").unsqueeze(2).broadcast_to([P, GE * HC, N]), ALU.add).then_inc(m["hid_biased"], 1)

            def finish(g, u):
                dve.wait_ge(m["out_done"], g + 3)
                for k in range(2):
                    last = dve.tensor_tensor(out_t[:, :, k, bass.ds(g * GE, GE)].rearrange("o n e -> o e n"), o_ps[u][:, 0:GE * N].rearrange("o (e n) -> o e n", n=N),
                                             b2_t[:, bass.ds(g * GE, GE)].unsqueeze(2).broadcast_to([P, GE, N]), ALU.add)
                last.then_inc(m["out_ready"], 1)

            for c in range(SLOTS // 4):
                dve.wait_ge(m["index_turned"], c + 1)
                dve.tensor_copy(index_row[:, 4 * c:4 * c + 4, :], a_ps[:, c].rearrange("p (c x) -> p c x", c=4)).then_inc(m["index_copied"], 1)
            dve.wait_ge(m["index_copied"], SLOTS // 4)
            dve.wait_ge(m["consts"], 5 + COLS)
            for n in range(N):
                every = index_row[:, n * COLS:(n + 1) * COLS, :].rearrange("p c x -> p (c x)")
                for q in range(COLS):
                    c = n * COLS + q
                    last = dve.tensor_scalar(equal[:, c, :], every, index[:, c:c + 1], None, ALU.is_equal)
                done(last)
                done(dve.tensor_tensor(first_only[:, :, :], equal[:, n * COLS:(n + 1) * COLS, :], earlier[:, :, :], ALU.mult))
                done(dve.tensor_reduce(dup[:, n * COLS:(n + 1) * COLS], first_only[:, :, :], AX_X, ALU.add))
            done(dve.tensor_scalar(dup[:, :], dup[:, :], 0.0, float(SKIP), ALU.is_gt, ALU.mult))
            done(dve.tensor_tensor(index_w[:, :], index[:, :], dup[:, :], ALU.add))
            done(dve.tensor_copy(index_wu[:, :], index_w[:, :]))

            GROUPS_E = EXPERTS // GE
            give(0, 0)
            give(1, 1)
            with dve.Fori(0, GROUPS_E // 2 - 1) as i:
                for u in range(2):
                    bias(2 * i + u, u)
                    give(2 * i + u + 2, u)
                    finish(2 * i + u, u)
            for u in range(2):
                bias(GROUPS_E - 2 + u, u)
                finish(GROUPS_E - 2 + u, u)
            for n in range(N):
                dve.wait_ge(m["out_turned"], n + 1)
                dve.tensor_tensor(weighted[:, n * COLS:(n + 1) * COLS, :], a_ps[:, n, 0:P].unsqueeze(1).broadcast_to([P, COLS, W]),
                                  weight[:, n * COLS:(n + 1) * COLS].unsqueeze(2).broadcast_to([P, COLS, W]), ALU.mult).then_inc(m["weighted_ready"], 1)
            for n in range(N):
                dve.wait_ge(m["summed"], n + 1)
                dve.tensor_tensor(result[:, n * COLS:(n + 1) * COLS, :], a_ps[:, n, :].rearrange("p (c x) -> p c x", c=COLS), rows[:, n * COLS:(n + 1) * COLS, :],
                                  ALU.add).then_inc(m["result_ready"], 1)

        @block.scalar
        def _(act):
            act.wait_ge(m["offs"], 3)
            act.activation(expo[:, :, :], off[:, :, :], ACT.Exp).then_inc(m["expd"], 1)
            ln.square(act, m["centred"], 1)
            ln.root(act, 0)
            with act.Fori(0, EXPERTS // GE // 2) as i:
                for u in range(2):
                    act.wait_ge(m["hid_biased"], 2 * i + u + 1)
                    act.activation(hid[u][:, :, :], hid_in[u][:, :, :], ACT.Gelu).then_inc(m["hid_ready"], 1)

        @block.tensor
        def _(pe):
            pe.sem_inc(m["hid_done"], 2)
            pe.wait_ge(m["ident_ready"], 1)
            pe.wait_ge(m["loaded"], 16 * 8)
            for c in range(HC):
                pe.transpose(a_ps[:, 0, c * EXPERTS:(c + 1) * EXPERTS], b1[:, c::HC], ident[0:EXPERTS, 0:EXPERTS])
            pe.transpose(a_ps[:, 0, HC * EXPERTS:(HC + 1) * EXPERTS], b2[:, :], ident[0:EXPERTS, 0:EXPERTS]).then_inc(m["bias_turned"], 1)
            pe.wait_ge(m["spread_ready"], 1)
            pe.wait_ge(m["bias_ready"], 1)
            for c in range(SLOTS):
                last = pe.transpose(a_ps[:, c // 4, (c % 4) * P:(c % 4 + 1) * P], spread[:, c, :], ident[:, :])
                if c % 4 == 3:
                    last.then_inc(m["index_turned"], 1)
            pe.wait_ge(m["scaled"], 1)
            pe.wait_ge(m["consts"], 5)
            for n in range(N):
                for q in range(COLS):
                    last = pe.matmul(p_ps[:, n * EXPERTS:(n + 1) * EXPERTS], tn[:, n * COLS + q, :], fold[:, :], start=q == 0, stop=q == COLS - 1)
            last.then_inc(m["pooled_done"], 1)

            def hidden(g, u):
                pe.wait_ge(w_loaded[u], 16 * g - 16 * u + 32)
                pe.wait_ge(m["group_ready"], g + 1)
                for e in range(GE):
                    for c in range(HC):
                        col = (e * HC + c) * N
                        last = pe.matmul(h_ps[u][:, col:col + N], w1[u][:, e, c::HC], pooled_g[u][:, e, :], start=True, stop=True)
                last.then_inc(m["hid_done"], 1)

            def outputs(g, u):
                pe.wait_ge(m["hid_ready"], g + 1)
                for e in range(GE):
                    for c in range(HC):
                        col = e * N
                        last = pe.matmul(o_ps[u][:, col:col + N], w2[u][:, e, c * W:(c + 1) * W], hid[u][:, e * HC + c, :], start=c == 0, stop=c == HC - 1)
                last.then_inc(m["out_done"], 1)

            with pe.Fori(0, EXPERTS // GE // 2) as i:
                for u in range(2):
                    hidden(2 * i + u, u)
                    outputs(2 * i + u, u)
            pe.wait_ge(m["out_ready"], EXPERTS // GE)
            pe.wait_ge(m["index_copied"], SLOTS // 4)
            for n in range(N):
                pe.transpose(a_ps[:, n, 0:P], out_t[:, n].rearrange("o k e -> o (k e)"), ident[:, :]).then_inc(m["out_turned"], 1)
            for n in range(N):
                pe.wait_ge(m["weighted_ready"], N)
                for q in range(COLS):
                    for t in range(COLS):
                        last = pe.matmul(a_ps[:, n, q * W:(q + 1) * W], equal[:, n * COLS + t, q * P:(q + 1) * P], weighted[:, n * COLS + t, :],
                                         start=t == 0, stop=t == COLS - 1)
                last.then_inc(m["summed"], 1)


PHASES = (prepare, project, attend, combine, experts)


def build(nc, d, phases=PHASES):
    def scratch(name, shape, dt=F32):
        d[name] = nc.dram_tensor(name, shape, dt, kind="Internal").ap()

    scratch("w_t", (4, C, C))
    scratch("r_parts", (2, PARTS, HD, NH, W * W), BF16)
    scratch("rv_t", (NH, W, W * HD))
    scratch("qk_parts", (PARTS, 2 * CHALF, P, N * PIX), BF16)
    scratch("v_t", (NCHUNK, NH, W, ROWS * HD))
    scratch("att_v", (N * 2, C, IHALF * W))
    scratch("att_r", (N * 2, C, QUADS, IHALF, JQ))
    scratch("cand", (N, P, TOPK))
    scratch("cand_at", (N, P, TOPK), U32)
    scratch("cand_sum", (N, P, 1))
    for phase in phases:
        phase(nc, d)


_INS = ["x", "L0_conv_wq", "L0_conv_wk", "L0_conv_wv", "L0_conv_wo", "L0_conv_rq", "L0_conv_rk", "L0_conv_rv",
        "L0_conv_Gq", "L0_conv_Gk", "L0_conv_Gv1", "L0_conv_Gv2",
        "L0_ffn_gate_w", "L0_ffn_gate_b", "L0_ffn_weight1", "L0_ffn_weight2"]


def kernel(**inputs):
    import numpy as _np
    import concourse.bacc as _bacc
    from concourse import mybir as _mybir
    from concourse.bass_utils import run_bass_kernel_spmd as _run

    nc = _bacc.Bacc("TRN2", target_bir_lowering=False, num_devices=1)
    arrays, d = {}, {}
    for name in _INS:
        a = _np.ascontiguousarray(inputs[name])
        arrays[f"in_{name}_dram"] = a
        short = name.replace("L0_conv_", "").replace("L0_ffn_", "")
        d[short] = nc.dram_tensor(f"in_{name}_dram", a.shape, _mybir.dt.from_np(a.dtype), kind="ExternalInput").ap()
    d["out"] = nc.dram_tensor("out_0_dram", (N, C, H, W), F32, kind="ExternalOutput").ap()
    build(nc, d)
    r = _run(nc, [arrays], core_ids=[0])
    return r.results[0]["out_0_dram"]
```
